# Optimizing a Trainium2 kernel written in Bass

```python
import numpy as np
import jax
import jax.numpy as jnp

def _softmax(x, axis=-1):
    return jax.nn.softmax(x, axis=axis)

def _gelu(x):
    return jax.nn.gelu(x, approximate=True)

def _silu(x):
    return jax.nn.silu(x)

def _sigmoid(x):
    return jax.nn.sigmoid(x)

def _layernorm(x, axis=-1, eps=1e-05):
    m = jnp.mean(x, axis=axis, keepdims=True)
    v = jnp.var(x, axis=axis, keepdims=True)
    return (x - m) / jnp.sqrt(v + eps)

def _scatter_add(tgt, idx, src, axis=0):
    return tgt.at[idx].add(src)

def _segment_sum(src, seg, n):
    return jax.ops.segment_sum(src, seg, n)
kernel_name = 'mk_gnn_preln_d2_gnn_r16_192b42'

def setup_inputs(seed: int=0):
    np.random.seed(seed)
    _w = jnp.asarray

    def _rec_inputs():
        import jax
        import jax.numpy as jnp
        _gk = jax.random.key(seed)
        x = -0.0006008 + 1.001 * jax.random.normal(jax.random.fold_in(_gk, 1), (3125, 256), jnp.float32)
        src = jax.random.randint(jax.random.fold_in(_gk, 2), (100000,), 0, 3125, jnp.int32)
        dst = jnp.minimum((3125 * jax.random.uniform(jax.random.fold_in(_gk, 3), (100000,)) ** 2.0).astype(jnp.int32), 49999)
        _o = jnp.argsort(dst, stable=True)
        src = src[_o]
        dst = dst[_o]
        edge_attr_64 = 0.000312547 + 1.00004 * jax.random.normal(jax.random.fold_in(_gk, 12), (100000, 64), jnp.float32)
        edge_type_16 = jax.random.randint(jax.random.fold_in(_gk, 14), (100000,), 0, 16, jnp.int32)
        return (x, src, dst, edge_attr_64, edge_type_16)
    x, src, dst, edge_attr_64, edge_type_16 = _rec_inputs()

    def _L0_gnn_setup():
        import jax, jax.numpy as jnp
        import numpy as np
        N, E, H, DE = (625, 15625, 256, 64)
        EPS = 1e-05

        def _lin_init(k, fan_in, shape):
            s = 1.0 / np.sqrt(fan_in)
            return jax.random.uniform(k, shape, jnp.float32, -s, s)
        key = jax.random.key(seed)
        ks = jax.random.split(key, 12)
        x = jax.random.normal(ks[0], (N, H), jnp.float32)
        edge_index = jax.random.randint(ks[1], (2, E), 0, N)
        edge_attr = jax.random.normal(ks[2], (E, DE), jnp.float32)
        d_in = H + DE
        W1 = _lin_init(ks[3], d_in, (d_in, H))
        b1 = _lin_init(ks[4], d_in, (H,))
        W2 = _lin_init(ks[5], H, (H, H))
        b2 = _lin_init(ks[6], H, (H,))
        Wg = _lin_init(ks[7], d_in, (d_in, H))
        bg = _lin_init(ks[8], d_in, (H,))
        gamma = jnp.ones((H,), jnp.float32)
        beta = jnp.zeros((H,), jnp.float32)
        return {'x': x, 'edge_index': edge_index, 'edge_attr': edge_attr, 'W1': W1, 'b1': b1, 'W2': W2, 'b2': b2, 'Wg': Wg, 'bg': bg, 'gamma': gamma, 'beta': beta}
    _L0_gnn_all = _L0_gnn_setup()
    _L0_gnn_in = {k: v for k, v in _L0_gnn_all.items() if k in ('W1', 'b1', 'W2', 'b2', 'Wg', 'bg', 'gamma', 'beta')}
    del _L0_gnn_all

    def _L1_gnn_setup():
        import jax, jax.numpy as jnp
        import numpy as np
        from jax.ops import segment_sum
        N_NODES = 625
        N_EDGES = 10000
        IN_FEAT = 256
        OUT_FEAT = 256
        NUM_RELS = 16

        def _inv_degree(idx, n):
            deg = segment_sum(jnp.ones(idx.shape[0], dtype=jnp.float32), idx, num_segments=n)
            return jnp.where(deg > 0, 1.0 / deg, 0.0)

        def _typed_pass(feat, W, bias, src_idx, dst_idx, etypes, norm_per_edge, n):
            proj = jnp.einsum('ni,rio->rno', feat, W)
            m = proj[etypes, src_idx] + bias
            m = m * norm_per_edge[:, None]
            return segment_sum(m, dst_idx, num_segments=n)
        key = jax.random.key(seed)
        ks = jax.random.split(key, 8)
        feat = jax.random.normal(ks[0], (N_NODES, IN_FEAT), dtype=jnp.float32)
        Wf = jax.random.normal(ks[1], (NUM_RELS, IN_FEAT, OUT_FEAT), dtype=jnp.float32)
        Wb = jax.random.normal(ks[2], (NUM_RELS, IN_FEAT, OUT_FEAT), dtype=jnp.float32)
        loop_weight = jax.random.normal(ks[3], (IN_FEAT, OUT_FEAT), dtype=jnp.float32)
        forward_bias = jnp.zeros((OUT_FEAT,), dtype=jnp.float32)
        backward_bias = jnp.zeros((OUT_FEAT,), dtype=jnp.float32)
        self_bias = jnp.zeros((OUT_FEAT,), dtype=jnp.float32)
        src = jax.random.randint(ks[4], (N_EDGES,), 0, N_NODES, dtype=jnp.int32)
        dst = jax.random.randint(ks[5], (N_EDGES,), 0, N_NODES, dtype=jnp.int32)
        etypes = jax.random.randint(ks[6], (N_EDGES,), 0, NUM_RELS, dtype=jnp.int32)
        return {'feat': feat, 'Wf': Wf, 'Wb': Wb, 'loop_weight': loop_weight, 'forward_bias': forward_bias, 'backward_bias': backward_bias, 'self_bias': self_bias, 'src': src, 'dst': dst, 'etypes': etypes, 'use_dis_weight': 0, 'drop_out': 0}
    _L1_gnn_all = _L1_gnn_setup()
    _L1_gnn_in = {k: v for k, v in _L1_gnn_all.items() if k in ('Wf', 'Wb', 'loop_weight', 'forward_bias', 'backward_bias', 'self_bias')}
    del _L1_gnn_all
    return {'x': x, 'src': src, 'dst': dst, 'edge_attr_64': edge_attr_64, 'edge_type_16': edge_type_16, 'L0_gnn_W1': _L0_gnn_in['W1'], 'L0_gnn_b1': _L0_gnn_in['b1'], 'L0_gnn_W2': _L0_gnn_in['W2'], 'L0_gnn_b2': _L0_gnn_in['b2'], 'L0_gnn_Wg': _L0_gnn_in['Wg'], 'L0_gnn_bg': _L0_gnn_in['bg'], 'L0_gnn_gamma': _L0_gnn_in['gamma'], 'L0_gnn_beta': _L0_gnn_in['beta'], 'L1_gnn_Wf': _L1_gnn_in['Wf'], 'L1_gnn_Wb': _L1_gnn_in['Wb'], 'L1_gnn_loop_weight': _L1_gnn_in['loop_weight'], 'L1_gnn_forward_bias': _L1_gnn_in['forward_bias'], 'L1_gnn_backward_bias': _L1_gnn_in['backward_bias'], 'L1_gnn_self_bias': _L1_gnn_in['self_bias']}

def reference(x, src, dst, edge_attr_64, edge_type_16, L0_gnn_W1, L0_gnn_b1, L0_gnn_W2, L0_gnn_b2, L0_gnn_Wg, L0_gnn_bg, L0_gnn_gamma, L0_gnn_beta, L1_gnn_Wf, L1_gnn_Wb, L1_gnn_loop_weight, L1_gnn_forward_bias, L1_gnn_backward_bias, L1_gnn_self_bias):
    import jax
    import jax.numpy as jnp

    def _L0_gnn_ref(x, edge_index, edge_attr, W1, b1, W2, b2, Wg, bg, gamma, beta):
        import jax, jax.numpy as jnp
        import numpy as np
        N, E, H, DE = (625, 15625, 256, 64)
        EPS = 1e-05

        def _lin_init(k, fan_in, shape):
            s = 1.0 / np.sqrt(fan_in)
            return jax.random.uniform(k, shape, jnp.float32, -s, s)
        src, dst = (edge_index[0], edge_index[1])
        ei = jnp.concatenate([x[src], edge_attr], axis=-1)
        core = jnp.maximum(ei @ W1 + b1, 0.0) @ W2 + b2
        gate = jax.nn.sigmoid(ei @ Wg + bg)
        msg = gate * core
        agg = jax.ops.segment_sum(msg, dst, num_segments=x.shape[0])
        out = agg + x
        mu = jnp.mean(out, axis=-1, keepdims=True)
        var = jnp.var(out, axis=-1, keepdims=True)
        out = (out - mu) * jax.lax.rsqrt(var + EPS) * gamma + beta
        return out

    def _L1_gnn_ref(feat, Wf, Wb, loop_weight, forward_bias, backward_bias, self_bias, src, dst, etypes, use_dis_weight, drop_out):
        import jax, jax.numpy as jnp
        import numpy as np
        from jax.ops import segment_sum
        N_NODES = 625
        N_EDGES = 10000
        IN_FEAT = 256
        OUT_FEAT = 256
        NUM_RELS = 16

        def _inv_degree(idx, n):
            deg = segment_sum(jnp.ones(idx.shape[0], dtype=jnp.float32), idx, num_segments=n)
            return jnp.where(deg > 0, 1.0 / deg, 0.0)

        def _typed_pass(feat, W, bias, src_idx, dst_idx, etypes, norm_per_edge, n):
            proj = jnp.einsum('ni,rio->rno', feat, W)
            m = proj[etypes, src_idx] + bias
            m = m * norm_per_edge[:, None]
            return segment_sum(m, dst_idx, num_segments=n)
        n = feat.shape[0]
        norm_f = _inv_degree(dst, n)[dst]
        m_forward = _typed_pass(feat, Wf, forward_bias, src, dst, etypes, norm_f, n)
        norm_b = _inv_degree(src, n)[src]
        m_backward = _typed_pass(feat, Wb, backward_bias, dst, src, etypes, norm_b, n)
        s = feat @ loop_weight
        s = s + s + self_bias
        return s + m_forward + m_backward
    edge_index = jnp.stack([src, dst])
    h = jnp.maximum(_layernorm(x, axis=-1), 0.0)
    x = x + _L0_gnn_ref(h, edge_index, edge_attr_64, L0_gnn_W1, L0_gnn_b1, L0_gnn_W2, L0_gnn_b2, L0_gnn_Wg, L0_gnn_bg, L0_gnn_gamma, L0_gnn_beta)
    h = jnp.maximum(_layernorm(x, axis=-1), 0.0)
    x = x + _L1_gnn_ref(h, L1_gnn_Wf, L1_gnn_Wb, L1_gnn_loop_weight, L1_gnn_forward_bias, L1_gnn_backward_bias, L1_gnn_self_bias, src, dst, edge_type_16, 0, 0)
    return x

_drawn_inputs = setup_inputs


def setup_inputs(seed=0):
    import zlib

    import numpy as np

    out = dict(_drawn_inputs(seed))
    spreads = {'L0_gnn_gamma': (1.0, 0.2),
     'L0_gnn_beta': (0.0, 0.1),
     'L1_gnn_forward_bias': (0.0, 0.8),
     'L1_gnn_backward_bias': (0.0, 0.8),
     'L1_gnn_self_bias': (0.0, 0.8)}
    factors = {'L0_gnn_bg': 6.03}
    for name, (base, spread) in spreads.items():
        noise = np.random.default_rng([zlib.crc32(name.encode()), seed]).standard_normal(out[name].shape)
        drawn = base * np.exp(spread * noise) if base else spread * noise
        out[name] = jnp.asarray(drawn.astype(out[name].dtype))
    for name, factor in factors.items():
        out[name] = (out[name] * factor).astype(out[name].dtype)
    return out
```

```python
import concourse.bass as bass
from concourse import mybir
from contextlib import ExitStack

F32 = mybir.dt.float32
I32 = mybir.dt.int32
ALU = mybir.AluOpType
ACT = mybir.ActivationFunctionType
AX = mybir.AxisListType
RMAX = bass.bass_isa.ReduceOp.max

P = 128
NODES, H, DE, RELS = 3125, 256, 64, 16
EDGES = 100000
NB = -(-NODES // P)
NPAD = NB * P
LAST = NODES - (NB - 1) * P
J = 4
SE = J * P
ST = -(-EDGES // SE)
COLS = ST * J
HK = H // P
AW = H + 2
NQ = RELS
EPS = 1e-5
NW = 14
assert ST % 2 == 0 and NQ % 2 == 0 and NB % 5 == 0


def gnn_program(nc, x, dst_l, src_l, typ_l, ea_t, W1, b1, W2, b2, Wg, bg, gamma, beta,
                Wrel, Wl, fbias, bbias, sbias, out):
    ptab = nc.dram_tensor("ptab", (NPAD, 2 * H), F32, kind="Internal").ap()
    proj = nc.dram_tensor("proj", (2 * RELS * NPAD, H), F32, kind="Internal").ap()
    byrec = nc.dram_tensor("byrec", (ST * SE, 2), I32, kind="Internal").ap()

    ctx = ExitStack()
    with ctx:
        def sb(name, shape, dt=F32):
            return ctx.enter_context(nc.sbuf_tensor(name, shape, dt))

        def pb(name, shape):
            return ctx.enter_context(nc.psum_tensor(name, shape, F32))

        def sem(name):
            return ctx.enter_context(nc.semaphore(name))

        res = sb("res", [P, NB, H])
        acc = sb("acc", [P, NB, AW])
        hT = sb("hT", [P, HK, NPAD])
        stats = sb("stats", [P, NB, 6])
        mv = sb("mv", [P, NB, 2])
        rstd = sb("rstd", [P, NB])
        nmr = sb("nmr", [P, NB])
        inv = sb("inv", [P, NB])
        ind = sb("ind", [P, NB])
        eps_t = sb("eps_t", [P, 1])
        wtop = sb("wtop", [P, HK, 2 * H])
        wbot = sb("wbot", [DE, 2 * H])
        w2 = sb("w2", [P, HK, H])
        wl = sb("wl", [P, HK, H])
        brow = sb("brow", [1, 2 * H])
        b2row = sb("b2row", [1, H])
        ones_row = sb("ones_row", [1, P])
        gamma_b = sb("gamma_b", [P, H])
        beta_b = sb("beta_b", [P, H])
        sbias_b = sb("sbias_b", [P, H])
        dbias_b = [sb(f"dbias_b{d}", [P, H]) for d in range(2)]
        ident = sb("ident", [P, P])
        tri = sb("tri", [P, P])
        ones_sq = sb("ones_sq", [P, P])
        dst_i = sb("dst_i", [P, COLS], I32)
        src_i = sb("src_i", [P, COLS], I32)
        typ_i = sb("typ_i", [P, COLS], I32)
        dst_f = sb("dst_f", [P, COLS])
        src_f = sb("src_f", [P, COLS])
        row_src = sb("row_src", [P, COLS], I32)
        pos_i = sb("pos_i", [P, COLS], I32)
        rec = sb("rec", [P, COLS, 2], I32)
        iota = sb("iota", [P, NPAD])
        win = [sb(f"win{k}", [1, 3 * ST], I32) for k in range(2)]
        pbuf = sb("pbuf", [P, 2, J, 2 * H])
        gbuf = pbuf[:, :, :, :].rearrange("p a j f -> p (a j f)")[:, 0:2 * J * AW].rearrange(
            "p (a j f) -> p a j f", a=2, j=J)
        ea = sb("ea", [DE, 2, SE])
        uT = sb("uT", [P, 2, HK, SE])
        gate = sb("gate", [P, 2, J, H])
        msg = sb("msg", [P, 2, J, H])
        onehot = sb("onehot", [P, 3, J, P])
        slot = sb("slot", [P, 2, J], I32)
        rslot = sb("rslot", [P, 2, J], I32)
        rrec = sb("rrec", [P, 2, J, 2], I32)
        iota_i = hT[:, 0, :].bitcast(I32)
        row_l0 = src_i
        tstage = pbuf
        wbuf = uT[:, :, :, :].rearrange("p a k (r f) -> p a k r f", r=2)
        pstage = [gate[:, 0, 0:2, :], gate[:, 0, 2:4, :], gate[:, 1, 0:2, :], gate[:, 1, 2:4, :], msg[:, 0, 0:2, :]]
        scr = [msg[:, :, :, :].rearrange("p a j f -> p (a j f)")[:, n * COLS:(n + 1) * COLS] for n in range(2)]
        scr += [gate[:, :, :, :].rearrange("p a j f -> p (a j f)")[:, n * COLS:(n + 1) * COLS] for n in range(2)]
        cnt = sb("cnt", [P, NB])
        off = sb("off", [P, NB])
        tot = sb("tot", [P, NB])
        ones_c = sb("ones_c", [P, COLS])
        wred = sb("wred", [P, 2, ST])
        wall = sb("wall", [P, 2, ST])
        wex = sb("wex", [1, 2, ST])

        pu = pb("pu", [P, HK, SE])
        pg = pb("pg", [P, J, H])
        pc = pb("pc", [P, J, H])
        pa = pb("pa", [P, 2, SE])
        pslots = [pu[:, 0, :], pu[:, 1, :], pg[:, 0:2, :].rearrange("p j f -> p (j f)"),
                  pg[:, 2:4, :].rearrange("p j f -> p (j f)"), pc[:, 0:2, :].rearrange("p j f -> p (j f)")]

        s_memset = sem("s_memset")
        s_x = sem("s_x")
        s_xlast = sem("s_xlast")
        s_idx = sem("s_idx")
        s_w = sem("s_w")
        s_xzero = sem("s_xzero")
        s_dve = sem("s_dve")
        s_pool = sem("s_pool")
        s_go = sem("s_go")
        s_var = [sem(f"s_var{k}") for k in range(3)]
        s_std = [sem(f"s_std{k}") for k in range(3)]
        s_norm = [sem(f"s_norm{k}") for k in range(3)]
        s_h = [sem(f"s_h{k}") for k in range(3)]
        s_tr = [sem(f"s_tr{k}") for k in range(2)]
        s_hT = [sem(f"s_hT{k}") for k in range(2)]
        s_tab = sem("s_tab")
        s_tabc = sem("s_tabc")
        s_tabst = [sem(f"s_tabst{k}") for k in range(2)]
        s_cnt = sem("s_cnt")
        s_tot = sem("s_tot")
        s_wmm = [sem(f"s_wmm{k}") for k in range(2)]
        s_wall = [sem(f"s_wall{k}") for k in range(2)]
        s_win = [sem(f"s_win{k}") for k in range(2)]
        s_pos = sem("s_pos")
        s_slot = sem("s_slot")
        s_gath = [[sem(f"s_gath{k}_{h}") for h in range(2)] for k in range(3)]
        s_scat = [sem(f"s_scat{k}") for k in range(2)]
        s_back = sem("s_back")
        s_back_f = sem("s_back_f")
        s_ea = [sem(f"s_ea{k}") for k in range(2)]
        s_u = sem("s_u")
        s_relu = sem("s_relu")
        s_g = sem("s_g")
        s_gsum = sem("s_gsum")
        s_gate = sem("s_gate")
        s_core = sem("s_core")
        s_msg = sem("s_msg")
        s_oh = [sem(f"s_oh{k}") for k in range(3)]
        s_agg = [sem(f"s_agg{k}") for k in range(3)]
        s_add = [sem(f"s_add{k}") for k in range(3)]
        s_xoh = [sem(f"s_xoh{k}") for k in range(3)]
        s_xadd = [sem(f"s_xadd{k}") for k in range(3)]
        s_xagg = [sem(f"s_xagg{k}") for k in range(3)]
        s_self = sem("s_self")
        s_selfadd = sem("s_selfadd")
        s_zero = [sem(f"s_zero{k}") for k in range(2)]
        s_wrel = [sem(f"s_wrel{k}") for k in range(2)]
        s_proj = sem("s_proj")
        s_pev = [sem(f"s_pev{k}") for k in range(5)]
        s_pst = [sem(f"s_pst{k}") for k in range(5)]
        s_g1 = [sem(f"s_g1_{k}") for k in range(2)]
        s_final = sem("s_final")
        s_out = sem("s_out")

        block = ctx.enter_context(nc.Block())

        def past(s, n):
            return not isinstance(s, int) or s >= n

        def evacuate(eng, copy, q, b):
            n = b % 5
            eng.wait_ge(s_proj, NB * q + b + 1)
            if b >= 5:
                eng.wait_ge(s_pst[n], 16 * (5 * q + b // 5))
            elif past(q, 1):
                eng.wait_ge(s_pst[n], 16 * 5 * q)
            copy(pstage[n].rearrange("p r f -> p (r f)"), pslots[n]).then_inc(s_pev[n], 1)

        def supertiles(eng):
            yield 0, 0, 0
            yield 1, 1, 0
            with eng.Fori(0, ST // 2 - 1) as i:
                yield 2 * i + 2, 0, i + 1
                yield 2 * i + 3, 1, i + 1

        def window(eng, k, s):
            w = win[k]
            lo = eng.value_load(w[0:1, bass.ds(3 * s, 1)], min_val=0, max_val=NB - 1)
            hi = eng.value_load(w[0:1, bass.ds(3 * s + 1, 1)], min_val=0, max_val=NB - 1)
            wx = eng.value_load(w[0:1, bass.ds(3 * s + 2, 1)], min_val=0, max_val=ST * NB)
            return lo, hi, wx

        def evacuate_pair(eng, copy, i, odd):
            for u in range(2):
                for b in range(NB):
                    if b % 5 % 2 == odd:
                        evacuate(eng, copy, 2 * i + u, b)

        @block.sync
        def _(sp):
            sp.dma_start(res[:, 0:NB - 1, :], x[0:(NB - 1) * P, :].rearrange("(b p) f -> p b f", p=P)).then_inc(s_x, 16)
            for t, a in ((dst_i, dst_l), (src_i, src_l), (typ_i, typ_l)):
                sp.dma_start(t[:, :], a).then_inc(s_idx, 16)
            for n, w in enumerate((W1, Wg)):
                sp.dma_start(wtop[:, :, n * H:(n + 1) * H], w[0:H, :].rearrange("(k p) f -> p k f", p=P)).then_inc(s_w, 16)
                sp.dma_start(wbot[:, n * H:(n + 1) * H], w[H:H + DE, :]).then_inc(s_w, 16)
            sp.dma_start(w2[:, :, :], W2.rearrange("(k p) f -> p k f", p=P)).then_inc(s_w, 16)
            sp.dma_start(wl[:, :, :], Wl.rearrange("(k p) f -> p k f", p=P)).then_inc(s_w, 16)
            sp.dma_start(brow[:, 0:H], b1).then_inc(s_w, 16)
            sp.dma_start(brow[:, H:2 * H], bg).then_inc(s_w, 16)
            sp.dma_start(b2row[:, :], b2).then_inc(s_w, 16)
            for t, a in ((gamma_b, gamma), (beta_b, beta), (sbias_b, sbias), (dbias_b[0], fbias), (dbias_b[1], bbias)):
                sp.dma_start(t[:, :], a.to_broadcast([P, H])).then_inc(s_w, 16)
            sp.wait_ge(s_xzero, 1)
            sp.dma_start(res[0:LAST, NB - 1, :], x[(NB - 1) * P:NODES, :]).then_inc(s_xlast, 16)
            for b in range(NB):
                sp.wait_ge(s_tabc, b + 1)
                sp.dma_start(ptab[b * P:(b + 1) * P, :], tstage[:, b % 2, 0, :]).then_inc(s_tabst[b % 2], 16)
            for s, par, pair in supertiles(sp):
                if past(s, 2):
                    sp.wait_ge(s_u, s - 1)
                    sp.wait_ge(s_g, s - 1)
                sp.dma_start(ea[:, par, :], ea_t[bass.ds(s, 1), :, :].rearrange("o d e -> (o d) e")).then_inc(s_ea[par], 16)
            for k in range(2):
                sp.wait_ge(s_scat[k], 16 * J * (ST // 2))
            sp.dma_start(rec[:, :, :].rearrange("p (s j) c -> p s (j c)", j=J),
                         byrec.rearrange("(s p j) c -> p s (j c)", p=P, j=J)).then_inc(s_back, 16)
            wv = Wrel.rearrange("(q r) (k p) f -> q p k r f", r=2, p=P)
            pv = proj.rearrange("(q r b p) f -> q p b r f", r=2, b=NB, p=P)

            def load_weights(q, par):
                for kk in range(HK):
                    sp.dma_start(wbuf[:, par, kk, :, :],
                                 wv[bass.ds(q, 1), :, kk, :, :].rearrange("q p r f -> (q p) r f")).then_inc(s_wrel[par], 16)

            def store_projections(q):
                for b in range(NB):
                    n = b % 5
                    sp.wait_ge(s_pev[n], 5 * q + b // 5 + 1)
                    sp.dma_start(pv[bass.ds(q, 1), :, b, :, :].rearrange("q p r f -> (q p) r f"),
                                 pstage[n]).then_inc(s_pst[n], 16)

            sp.wait_ge(s_core, ST)
            load_weights(0, 0)
            load_weights(1, 1)
            with sp.Fori(0, NQ // 2 - 1) as i:
                for u in range(2):
                    q = 2 * i + u
                    store_projections(q)
                    sp.wait_ge(s_proj, NB * (q + 1))
                    load_weights(q + 2, u)
            store_projections(NQ - 2)
            store_projections(NQ - 1)
            for n in range(5):
                sp.wait_ge(s_pst[n], 16 * 5 * NQ)
            sp.wait_ge(s_final, 1)
            sp.dma_start(out[0:(NB - 1) * P, :].rearrange("(b p) f -> p b f", p=P), res[:, 0:NB - 1, :]).then_inc(s_out, 16)
            sp.dma_start(out[(NB - 1) * P:NODES, :], res[0:LAST, NB - 1, :]).then_inc(s_out, 16)
            sp.wait_ge(s_out, 32)

        @block.gpsimd
        def _(pool):
            nc.gpsimd.iota(iota_i, pattern=[[1, NPAD]], base=0, channel_multiplier=0)
            nc.gpsimd.memset(ident[:, :], 0.0)
            nc.gpsimd.memset(tri[:, :], 1.0)
            nc.gpsimd.memset(ones_sq[:, :], 1.0)
            nc.gpsimd.memset(ones_row[:, :], 1.0).then_inc(s_pool, 1)
            pool.wait_ge(s_pool, 1)
            nc.gpsimd.affine_select(out=ident[:, :], in_=ident[:, :], compare_op=ALU.not_equal, fill=1.0,
                                    base=0, pattern=[[-1, P]], channel_multiplier=1)
            nc.gpsimd.affine_select(out=tri[:, :], in_=tri[:, :], compare_op=ALU.is_gt, fill=0.0,
                                    base=0, pattern=[[1, P]], channel_multiplier=-1).then_inc(s_memset, 1)

            def reduce_windows(k):
                pool.wait_ge(s_wmm[k], 1)
                nc.gpsimd.partition_all_reduce(wall[:, :, :].rearrange("p a s -> p (a s)"),
                                               wred[:, :, :].rearrange("p a s -> p (a s)"), P, RMAX).then_inc(s_wall[k], 1)

            def take_indices(k, s, par, col):
                nc.gpsimd.tensor_copy(slot[:, par, :], col).then_inc(s_slot, 1)

            for k in range(3):
                for c in (s_xoh[k], s_xagg[k], s_xadd[k]):
                    pool.sem_inc(c, NB)
            reduce_windows(0)
            for k in range(2):
                pool.wait_ge(s_tabst[k], 16 * ((NB + 1 - k) // 2))
            pool.wait_ge(s_pos, 1)
            for s, par, pair in supertiles(pool):
                if past(s, 2):
                    pool.wait_ge(s_u, s - 1)
                    pool.wait_ge(s_gsum, s - 1)
                    pool.wait_ge(s_scat[par], 16 * J * pair)
                cols = bass.ds(J * s, J)
                nc.gpsimd.tensor_copy(slot[:, par, :], row_l0[:, cols])
                nc.gpsimd.tensor_copy(rslot[:, par, :], pos_i[:, cols])
                nc.gpsimd.tensor_copy(rrec[:, par, :, :], rec[:, cols, :]).then_inc(s_slot, 1)
                pool.wait_ge(s_slot, s + 1)
                pool.sem_inc(s_go, 1)
                for j in range(J):
                    pool.indirect_dma_start(pbuf[:, par, j, :], None, ptab[:, :],
                                            bass.IndirectOffsetOnAxis(ap=slot[:, par, j:j + 1], axis=0)
                                            ).then_inc(s_gath[0][par], 16)
                for j in range(J):
                    pool.indirect_dma_start(byrec[:, :], bass.IndirectOffsetOnAxis(ap=rslot[:, par, j:j + 1], axis=0),
                                            rrec[:, par, j, :], None).then_inc(s_scat[par], 16)
            reduce_windows(1)
            for n in range(5):
                pool.wait_ge(s_pst[n], 16 * 5 * NQ)
            pool.wait_ge(s_zero[0], 1)
            for k in (1, 2):
                table = row_src[:, :] if k == 1 else rec[:, :, 0]
                for s, par, pair in supertiles(pool):
                    if past(s, 2):
                        pool.wait_ge(s_add[k], s - 1)
                    elif k == 2:
                        pool.wait_ge(s_add[1], ST)
                    nc.gpsimd.tensor_copy(slot[:, par, :], table[:, bass.ds(J * s, J)]).then_inc(s_slot, 1)
                    pool.wait_ge(s_slot, k * ST + s + 1)
                    pool.sem_inc(s_go, 1)
                    for j in range(J):
                        pool.indirect_dma_start(gbuf[:, par, j, 0:H], None, proj[:, :],
                                                bass.IndirectOffsetOnAxis(ap=slot[:, par, j:j + 1], axis=0)
                                                ).then_inc(s_gath[k][par], 16)

        @block.scalar
        def _(act):
            def sqrt_var(k):
                act.wait_ge(s_var[k], 1)
                nc.scalar.activation(rstd[:, :], mv[:, :, 1], ACT.Sqrt, bias=eps_t[:, 0:1]).then_inc(s_std[k], 1)

            def normalise(k, src, func):
                act.wait_ge(s_norm[k], 1)
                for b in range(NB):
                    nc.scalar.activation(acc[:, b, 0:H], src[:, b, 0:H], func, bias=nmr[:, b:b + 1],
                                         scale=rstd[:, b:b + 1]).then_inc(s_h[k], 1)

            sqrt_var(0)
            normalise(0, res, ACT.Relu)
            for b in range(NB):
                act.wait_ge(s_tab, b + 1)
                if b >= 2:
                    act.wait_ge(s_tabst[b % 2], 16 * (b // 2))
                nc.scalar.activation(tstage[:, b % 2, 0, :], pu[:, b % 2, :], ACT.Copy).then_inc(s_tabc, 1)
            for s, par, pair in supertiles(act):
                act.wait_ge(s_u, s + 1)
                if past(s, 2):
                    act.wait_ge(s_core, s - 1)
                for k in range(HK):
                    last = nc.scalar.activation(uT[:, par, k, :], pu[:, k, :], ACT.Relu)
                last.then_inc(s_relu, 1)
                act.wait_ge(s_gsum, s + 1)
                nc.scalar.activation(gate[:, par, :, :], gate[:, par, :, :], ACT.Sigmoid).then_inc(s_gate, 1)
            sqrt_var(1)
            normalise(1, acc, ACT.Identity)
            sqrt_var(2)
            normalise(2, res, ACT.Relu)
            evacuate_pair(act, nc.scalar.copy, 0, 0)
            with act.Fori(1, NQ // 2) as i:
                evacuate_pair(act, nc.scalar.copy, i, 0)

        @block.tensor
        def _(pe):
            def transposes(k, b):
                pe.wait_ge(s_h[2 * k], b + 1)
                if b >= 2:
                    pe.wait_ge(s_hT[k], b - 1)
                for kk in range(HK):
                    last = nc.tensor.transpose(pa[:, b % 2, kk * P:(kk + 1) * P], acc[:, b, kk * P:(kk + 1) * P], ident[:, :])
                last.then_inc(s_tr[k], 1)

            def table(b):
                pe.wait_ge(s_hT[0], b + 1)
                if b >= 2:
                    pe.wait_ge(s_tabc, b - 1)
                for kk in range(HK):
                    nc.tensor.matmul(pu[:, b % 2, :], hT[:, kk, b * P:(b + 1) * P], wtop[:, kk, :], start=(kk == 0), stop=False)
                nc.tensor.matmul(pu[:, b % 2, :], ones_row[:, :], brow[:, :], start=False, stop=True).then_inc(s_tab, 1)

            def own(b):
                pe.wait_ge(s_hT[1], b + 1)
                if b >= 2:
                    pe.wait_ge(s_selfadd, b - 1)
                for kk in range(HK):
                    last = nc.tensor.matmul(pu[:, b % 2, 0:H], hT[:, kk, b * P:(b + 1) * P], wl[:, kk, :],
                                            start=(kk == 0), stop=(kk == HK - 1))
                last.then_inc(s_self, 1)

            pe.wait_ge(s_memset, 1)
            transposes(0, 0)
            pe.wait_ge(s_w, 16 * NW)
            for b in range(NB):
                if b + 1 < NB:
                    transposes(0, b + 1)
                table(b)
            pe.wait_ge(s_cnt, 1)
            nc.tensor.matmul(pg[:, 0, 0:NB], tri[:, :], cnt[:, :], start=True, stop=True)
            nc.tensor.matmul(pc[:, 0, 0:NB], ones_sq[:, :], cnt[:, :], start=True, stop=True).then_inc(s_tot, 1)
            pe.wait_ge(s_tabc, NB)
            pe.wait_ge(s_pos, 1)

            def edge_products(s, par, pair):
                pe.wait_ge(s_ea[par], 16 * (pair + 1))
                if past(s, 1):
                    pe.wait_ge(s_gsum, s)
                for j in range(J):
                    last = nc.tensor.matmul(pg[:, j, :], ea[:, par, j * P:(j + 1) * P], wbot[:, H:2 * H], start=True, stop=True)
                last.then_inc(s_g, 1)
                if past(s, 1):
                    pe.wait_ge(s_relu, s)
                pe.wait_ge(s_gath[0][par], 16 * J * (pair + 1))
                for kk in range(HK):
                    nc.tensor.matmul(pu[:, kk, :], wbot[:, kk * P:(kk + 1) * P], ea[:, par, :], start=True, stop=False)
                    for j in range(J):
                        last = nc.tensor.matmul(pu[:, kk, j * P:(j + 1) * P], pbuf[:, par, j, kk * P:(kk + 1) * P],
                                                ident[:, :], is_transpose=True, start=False, stop=(j == J - 1))
                last.then_inc(s_u, 1)

            def core(s, par):
                pe.wait_ge(s_relu, s + 1)
                if past(s, 1):
                    pe.wait_ge(s_msg, s)
                for j in range(J):
                    for kk in range(HK):
                        nc.tensor.matmul(pc[:, j, :], uT[:, par, kk, j * P:(j + 1) * P], w2[:, kk, :], start=(kk == 0), stop=False)
                    last = nc.tensor.matmul(pc[:, j, :], ones_row[:, :], b2row[:, :], start=False, stop=True)
                last.then_inc(s_core, 1)

            def sum_edges(k, s, par, pair, rows, width):
                lo, hi, wx = window(pe, k // 2, s)
                pe.wait_ge(s_oh[k], s + 1)
                if k == 0:
                    pe.wait_ge(s_msg, s + 1)
                else:
                    pe.wait_ge(s_gath[k][par], 16 * J * (pair + 1))
                if past(s, 2):
                    pe.wait_ge(s_add[k], s - 1)
                for j in range(J):
                    last = nc.tensor.matmul(pa[:, par, 0:width], onehot[:, par, j, :], rows[:, par, j, :],
                                            start=(j == 0), stop=(j == J - 1))
                last.then_inc(s_agg[k], 1)
                with pe.If(hi > lo):
                    with pe.Fori(lo + 1, hi + 1) as b:
                        pe.wait_ge(s_xoh[k], wx + b)
                        for j in range(J):
                            last = nc.tensor.matmul(pa[:, 1 - par, 0:width], onehot[:, 2, j, :], rows[:, par, j, :],
                                                    start=(j == 0), stop=(j == J - 1))
                        last.then_inc(s_xagg[k], 1)
                        pe.wait_ge(s_xadd[k], wx + b)

            edge_products(0, 0, 0)
            edge_products(1, 1, 0)
            core(0, 0)

            def l0_pair(i):
                for u in range(2):
                    edge_products(2 * i + u, u, i)
                    core(2 * i - 1 + u, 1 - u)
                    sum_edges(0, 2 * i - 2 + u, u, i - 1, msg, H)

            l0_pair(1)
            with pe.Fori(2, ST // 2) as i:
                l0_pair(i)
            core(ST - 1, 1)
            sum_edges(0, ST - 2, 0, 0, msg, H)
            sum_edges(0, ST - 1, 1, 0, msg, H)

            transposes(1, 0)
            for b in range(NB):
                if b + 1 < NB:
                    transposes(1, b + 1)
                own(b)
            pe.wait_ge(s_selfadd, NB)
            def project(i):
                for u in range(2):
                    q = 2 * i + u
                    pe.wait_ge(s_wrel[u], 16 * HK * (i + 1))
                    for b in range(NB):
                        n = b % 5
                        if b >= 5 or past(q, 1):
                            pe.wait_ge(s_pev[n], 5 * q + b // 5)
                        for kk in range(HK):
                            last = nc.tensor.matmul(pslots[n], hT[:, kk, b * P:(b + 1) * P],
                                                    wbuf[:, u, kk, :, :].rearrange("p r f -> p (r f)"),
                                                    start=(kk == 0), stop=(kk == HK - 1))
                        last.then_inc(s_proj, 1)
            project(0)
            with pe.Fori(1, NQ // 2) as i:
                project(i)
            for k in (1, 2):
                if k == 2:
                    pe.wait_ge(s_add[1], ST)
                for s, par, pair in supertiles(pe):
                    sum_edges(k, s, par, pair, gbuf, AW)

        @block.vector
        def _(dve):
            n_link = [0]

            def link(ins):
                n_link[0] += 1
                ins.then_inc(s_dve, 1)
                dve.wait_ge(s_dve, n_link[0])

            def ln_statistics(k, src):
                for b in range(NB):
                    last = nc.vector.bn_stats(stats[:, b, :], src[:, b, 0:H])
                link(last)
                for b in range(NB):
                    last = nc.vector.bn_aggr(mv[:, b, :], stats[:, b, :])
                last.then_inc(s_var[k], 1)
                dve.wait_ge(s_std[k], 1)
                link(nc.vector.reciprocal(rstd[:, :], rstd[:, :]))
                nc.vector.scalar_tensor_tensor(out=nmr[:, :], in0=mv[:, :, 0], scalar=-1.0, in1=rstd[:, :],
                                               op0=ALU.mult, op1=ALU.mult).then_inc(s_norm[k], 1)

            def evacuate_hT(k, b):
                dve.wait_ge(s_tr[k], b + 1)
                nc.vector.tensor_copy(hT[:, :, b * P:(b + 1) * P],
                                      pa[:, b % 2, 0:H].rearrange("p (k n) -> p k n", k=HK)).then_inc(s_hT[k], 1)

            def add_own(b):
                dve.wait_ge(s_self, b + 1)
                last = nc.vector.scalar_tensor_tensor(out=res[:, b, :], in0=pu[:, b % 2, 0:H], scalar=2.0,
                                                      in1=res[:, b, :], op0=ALU.mult, op1=ALU.add)
                last.then_inc(s_selfadd, 1)

            def window_extremes(k, blk):
                v = blk.rearrange("p (s j) -> p s j", j=J)
                nc.vector.tensor_reduce(wred[:, 0, :], v, AX.X, ALU.max)
                link(nc.vector.tensor_reduce(wred[:, 1, :], v, AX.X, ALU.min))
                nc.vector.tensor_scalar(wred[:, 1, :], wred[:, 1, :], -1.0, None, ALU.mult).then_inc(s_wmm[k], 1)

            def windows(k):
                dve.wait_ge(s_wall[k], 1)
                w = win[k][:, :].rearrange("o (s c) -> o s c", c=3)
                nc.vector.tensor_scalar(w[:, :, 0], wall[0:1, 1, :], -1.0, None, ALU.mult)
                nc.vector.tensor_copy(w[:, :, 1], wall[0:1, 0, :])
                link(nc.vector.tensor_tensor(wex[:, 0, :], wall[0:1, 0, :], wall[0:1, 1, :], ALU.add))
                link(nc.vector.tensor_tensor_scan(wex[:, 1, :], ones_c[0:1, 0:ST], wex[:, 0, :], 0.0, ALU.mult, ALU.add))
                link(nc.vector.tensor_tensor(wex[:, 1, :], wex[:, 1, :], wex[:, 0, :], ALU.subtract))
                nc.vector.scalar_tensor_tensor(out=w[:, :, 2], in0=wex[:, 1, :], scalar=float(NB), in1=wall[0:1, 1, :],
                                               op0=ALU.add, op1=ALU.add).then_inc(s_win[k], 1)

            nc.vector.memset(res[:, NB - 1, :], 0.0).then_inc(s_xzero, 1)
            nc.vector.memset(eps_t[:, :], EPS)
            link(nc.vector.memset(ones_c[:, :], 1.0))
            dve.wait_ge(s_x, 16)
            dve.wait_ge(s_xlast, 16)
            ln_statistics(0, res)

            dve.wait_ge(s_memset, 1)
            link(nc.vector.tensor_copy(iota[:, :], iota_i))

            blk_i = rec[:, :, 1]
            dve.wait_ge(s_idx, 48)
            nc.vector.tensor_copy(dst_f[:, :], dst_i[:, :])
            nc.vector.tensor_copy(src_f[:, :], src_i[:, :])
            nc.vector.tensor_copy(scr[1], typ_i[:, :])
            link(nc.vector.tensor_scalar(blk_i, dst_i[:, :], 7, None, ALU.logical_shift_right))
            nc.vector.tensor_copy(scr[0], blk_i)
            link(nc.vector.tensor_scalar(scr[1], scr[1], float(NPAD), None, ALU.mult))
            window_extremes(0, scr[0])
            nc.vector.tensor_tensor(row_src[:, :], scr[1], src_f[:, :], ALU.add)
            link(nc.vector.scalar_tensor_tensor(out=rec[:, :, 0], in0=scr[1], scalar=float(RELS * NPAD), in1=dst_f[:, :],
                                                op0=ALU.add, op1=ALU.add))
            for b in range(NB):
                evacuate_hT(0, b)
            windows(0)

            blk, eq, run, pos = scr[0], scr[1], scr[2], scr[3]
            link(nc.vector.tensor_scalar(blk_i, src_i[:, :], 7, None, ALU.logical_shift_right))
            link(nc.vector.tensor_copy(blk, blk_i))
            for b in range(NB):
                link(nc.vector.tensor_scalar(eq, blk, float(b), None, ALU.is_equal))
                link(nc.vector.tensor_reduce(cnt[:, b:b + 1], eq, AX.X, ALU.add))
            nc.vector.tensor_copy(rec[:, :, 1], src_i[:, :]).then_inc(s_cnt, 1)
            dve.wait_ge(s_tot, 1)
            link(nc.vector.tensor_copy(tot[:, :], pc[:, 0, 0:NB]))
            link(nc.vector.tensor_tensor_scan(off[:, :], ones_c[:, 0:NB], tot[:, :], 0.0, ALU.mult, ALU.add))
            link(nc.vector.tensor_tensor(off[:, :], off[:, :], tot[:, :], ALU.subtract))
            link(nc.vector.tensor_tensor(off[:, :], off[:, :], pg[:, 0, 0:NB], ALU.add))
            link(nc.vector.memset(pos, -1.0))
            for b in range(NB):
                link(nc.vector.tensor_scalar(eq, blk, float(b), None, ALU.is_equal))
                link(nc.vector.tensor_tensor_scan(run, ones_c[:, :], eq, off[:, b:b + 1], ALU.mult, ALU.add))
                link(nc.vector.tensor_tensor(run, run, eq, ALU.mult))
                link(nc.vector.tensor_tensor(pos, pos, run, ALU.add))
            nc.vector.tensor_copy(pos_i[:, :], pos).then_inc(s_pos, 1)

            def add_gathered(s, par, pair):
                dve.wait_ge(s_g, s + 1)
                dve.wait_ge(s_gath[0][par], 16 * J * (pair + 1))
                if past(s, 2):
                    dve.wait_ge(s_gate, s - 1)
                    dve.wait_ge(s_msg, s - 1)
                nc.vector.tensor_tensor(gate[:, par, :, :], pg[:, :, :], pbuf[:, par, :, H:2 * H], ALU.add).then_inc(s_gsum, 1)

            def one_hot(k, s, par, keys):
                lo, hi, wx = window(dve, k // 2, s)
                if past(s, 2):
                    dve.wait_ge(s_agg[k], s - 1)
                compare(par, lo, s, keys).then_inc(s_oh[k], 1)

            def compare(at, b, s, keys):
                nodes = iota[:, bass.ds(b * P, P)].unsqueeze(1).to_broadcast([P, J, P])
                own_keys = keys[:, bass.ds(J * s, J)].unsqueeze(2).to_broadcast([P, J, P])
                return nc.vector.tensor_tensor(onehot[:, at, :, :], nodes, own_keys, ALU.is_equal)

            def messages(s, par):
                dve.wait_ge(s_core, s + 1)
                dve.wait_ge(s_gate, s + 1)
                if past(s, 2):
                    dve.wait_ge(s_add[0], s - 1)
                nc.vector.tensor_tensor(msg[:, par, :, :], gate[:, par, :, :], pc[:, :, :], ALU.mult).then_inc(s_msg, 1)

            def add_sums(k, s, par, keys, width):
                lo, hi, wx = window(dve, k // 2, s)
                with dve.If(hi > lo):
                    with dve.Fori(lo + 1, hi + 1) as b:
                        if past(s, 1):
                            dve.wait_ge(s_add[k], s)
                        dve.wait_ge(s_xadd[k], wx + b - 1)
                        compare(2, b, s, keys).then_inc(s_xoh[k], 1)
                        dve.wait_ge(s_xagg[k], wx + b)
                        t = acc[:, bass.ds(b, 1), 0:width].rearrange("p o f -> p (o f)")
                        nc.vector.tensor_tensor(t, t, pa[:, 1 - par, 0:width], ALU.add).then_inc(s_xadd[k], 1)
                dve.wait_ge(s_xadd[k], wx + hi)
                if past(s, 1):
                    dve.wait_ge(s_add[k], s)
                dve.wait_ge(s_agg[k], s + 1)
                t = acc[:, bass.ds(lo, 1), 0:width].rearrange("p o f -> p (o f)")
                nc.vector.tensor_tensor(t, t, pa[:, par, 0:width], ALU.add).then_inc(s_add[k], 1)

            dve.wait_ge(s_win[0], 1)
            add_gathered(0, 0, 0)
            add_gathered(1, 1, 0)
            messages(0, 0)
            one_hot(0, 0, 0, dst_f)

            def l0_pair(i):
                for u in range(2):
                    add_gathered(2 * i + u, u, i)
                    messages(2 * i - 1 + u, 1 - u)
                    one_hot(0, 2 * i - 1 + u, 1 - u, dst_f)
                    add_sums(0, 2 * i - 2 + u, u, dst_f, H)

            l0_pair(1)
            with dve.Fori(2, ST // 2) as i:
                l0_pair(i)
            messages(ST - 1, 1)
            one_hot(0, ST - 1, 1, dst_f)
            add_sums(0, ST - 2, 0, dst_f, H)
            add_sums(0, ST - 1, 1, dst_f, H)
            dve.wait_ge(s_add[0], ST)

            ln_statistics(1, acc)
            a, g = acc[:, :, 0:H], lambda t: t[:, :].unsqueeze(1).to_broadcast([P, NB, H])
            dve.wait_ge(s_h[1], NB)
            link(nc.vector.tensor_tensor(a, a, g(gamma_b), ALU.mult))
            link(nc.vector.tensor_tensor(a, a, g(beta_b), ALU.add))
            link(nc.vector.tensor_tensor(res[:, :, :], res[:, :, :], a, ALU.add))
            ln_statistics(2, res)

            dve.wait_ge(s_back, 16)
            link(nc.vector.tensor_copy(src_f[:, :], rec[:, :, 1]))
            link(nc.vector.tensor_scalar(typ_i[:, :], rec[:, :, 1], 7, None, ALU.logical_shift_right))
            link(nc.vector.tensor_copy(scr[0], typ_i[:, :]))
            window_extremes(1, scr[0])
            for b in range(NB):
                evacuate_hT(1, b)
                if b >= 1:
                    add_own(b - 1)
            add_own(NB - 1)
            dve.wait_ge(s_selfadd, NB)
            link(nc.vector.tensor_tensor(res[:, :, :], res[:, :, :], g(sbias_b), ALU.add))
            windows(1)
            link(nc.vector.memset(acc[:, :, :], 0.0))
            nc.vector.memset(gbuf[:, :, :, H:AW], 1.0).then_inc(s_zero[0], 1)
            evacuate_pair(dve, nc.vector.tensor_copy, 0, 1)
            with dve.Fori(1, NQ // 2) as i:
                evacuate_pair(dve, nc.vector.tensor_copy, i, 1)
            for k in (1, 2):
                keys = dst_f if k == 1 else src_f
                one_hot(k, 0, 0, keys)
                one_hot(k, 1, 1, keys)
                add_sums(k, 0, 0, keys, AW)
                with dve.Fori(0, ST // 2 - 1) as i:
                    for u in range(2):
                        one_hot(k, 2 * i + 2 + u, u, keys)
                        add_sums(k, 2 * i + 1 + u, 1 - u, keys, AW)
                add_sums(k, ST - 1, 1, keys, AW)
                dve.wait_ge(s_add[k], ST)
                deg = acc[:, :, H]
                nc.vector.tensor_scalar(ind[:, :], deg, 1.0, None, ALU.min)
                link(nc.vector.tensor_scalar(inv[:, :], deg, 1.0, None, ALU.max))
                link(nc.vector.reciprocal(inv[:, :], inv[:, :]))
                for b in range(NB):
                    last = nc.vector.scalar_tensor_tensor(out=res[:, b, :], in0=acc[:, b, 0:H], scalar=inv[:, b:b + 1],
                                                          in1=res[:, b, :], op0=ALU.mult, op1=ALU.add)
                link(last)
                for b in range(NB):
                    last = nc.vector.scalar_tensor_tensor(out=res[:, b, :], in0=dbias_b[k - 1][:, :], scalar=ind[:, b:b + 1],
                                                          in1=res[:, b, :], op0=ALU.mult, op1=ALU.add)
                link(last)
                if k == 1:
                    link(nc.vector.memset(acc[:, :, :], 0.0))
            nc.vector.tensor_copy(ind[:, :], inv[:, :]).then_inc(s_final, 1)


_INS = ['x', 'dst_l', 'src_l', 'typ_l', 'ea_t', 'W1', 'b1', 'W2', 'b2', 'Wg', 'bg', 'gamma', 'beta',
        'Wrel', 'Wl', 'fbias', 'bbias', 'sbias']


def kernel(**inputs):
    import numpy as np
    import concourse.bacc as bacc
    from concourse.bass_utils import run_bass_kernel_spmd

    def order(a, fill):
        a = np.asarray(a)
        full = np.full((ST * SE,) + a.shape[1:], fill, a.dtype)
        full[:EDGES] = a
        return full.reshape((ST, P, J) + a.shape[1:])

    named = {"x": inputs["x"]}
    for name, key, fill in (("dst_l", "dst", NPAD - 1), ("src_l", "src", NPAD - 1), ("typ_l", "edge_type_16", 0)):
        named[name] = order(inputs[key], fill).transpose(1, 0, 2).reshape(P, COLS)
    named["ea_t"] = order(inputs["edge_attr_64"], 0).transpose(0, 3, 2, 1).reshape(ST, DE, SE)
    for name in ("W1", "W2", "Wg"):
        named[name] = inputs["L0_gnn_" + name]
    for name in ("b1", "b2", "bg", "gamma", "beta"):
        named[name] = np.asarray(inputs["L0_gnn_" + name]).reshape(1, H)
    named["Wrel"] = np.concatenate([np.asarray(inputs["L1_gnn_Wf"]), np.asarray(inputs["L1_gnn_Wb"])])
    named["Wl"] = inputs["L1_gnn_loop_weight"]
    for name, key in (("fbias", "forward_bias"), ("bbias", "backward_bias"), ("sbias", "self_bias")):
        named[name] = np.asarray(inputs["L1_gnn_" + key]).reshape(1, H)

    nc = bacc.Bacc("TRN2", target_bir_lowering=False, num_devices=1)
    arrays, args = {}, []
    for name in _INS:
        a = np.ascontiguousarray(named[name])
        arrays["in_" + name] = a
        args.append(nc.dram_tensor("in_" + name, a.shape, mybir.dt.from_np(a.dtype), kind="ExternalInput").ap())
    args.append(nc.dram_tensor("out_0", (NODES, H), F32, kind="ExternalOutput").ap())
    gnn_program(nc, *args)
    r = run_bass_kernel_spmd(nc, [arrays], core_ids=[0])
    return r.results[0]["out_0"]
```
